# Optimizing a Trainium2 kernel written in Bass

```python
import numpy as np
import jax
import jax.numpy as jnp

def _softmax(x, axis=-1):
    return jax.nn.softmax(x, axis=axis)

def _gelu(x):
    return jax.nn.gelu(x, approximate=True)

def _silu(x):
    return jax.nn.silu(x)

def _sigmoid(x):
    return jax.nn.sigmoid(x)

def _layernorm(x, axis=-1, eps=1e-05):
    m = jnp.mean(x, axis=axis, keepdims=True)
    v = jnp.var(x, axis=axis, keepdims=True)
    return (x - m) / jnp.sqrt(v + eps)

def _scatter_add(tgt, idx, src, axis=0):
    return tgt.at[idx].add(src)

def _segment_sum(src, seg, n):
    return jax.ops.segment_sum(src, seg, n)
kernel_name = 'mk_dlrm_tower_d1_rec_r8_f451dc'

def setup_inputs(seed: int=0):
    np.random.seed(seed)
    _w = jnp.asarray

    def _rec_inputs():
        import jax
        import jax.numpy as jnp
        _tk = jax.random.key(seed)
        dense_ctx = jax.random.normal(jax.random.fold_in(_tk, 190), (512, 16), jnp.float32)
        ids = jnp.stack([jax.random.randint(jax.random.fold_in(_tk, 200 + f), (512,), 0, v, jnp.int32) for f, v in enumerate([1000, 1250, 1000, 1250, 125000, 1250, 1250, 12500, 12500, 1000, 12500, 1000, 1250, 1250, 1000, 1250, 12500, 1250, 12500, 12500, 1250, 1000, 1250, 1250, 1000, 12500, 1000])], axis=1)
        tbl_0 = 0.05 * jax.random.normal(jax.random.fold_in(_tk, 500 + 0), (1000, 128), jnp.float32)
        tbl_1 = 0.05 * jax.random.normal(jax.random.fold_in(_tk, 500 + 1), (1250, 128), jnp.float32)
        tbl_2 = 0.05 * jax.random.normal(jax.random.fold_in(_tk, 500 + 2), (1000, 128), jnp.float32)
        tbl_3 = 0.05 * jax.random.normal(jax.random.fold_in(_tk, 500 + 3), (1250, 128), jnp.float32)
        tbl_4 = 0.05 * jax.random.normal(jax.random.fold_in(_tk, 500 + 4), (125000, 128), jnp.float32)
        tbl_5 = 0.05 * jax.random.normal(jax.random.fold_in(_tk, 500 + 5), (1250, 128), jnp.float32)
        tbl_6 = 0.05 * jax.random.normal(jax.random.fold_in(_tk, 500 + 6), (1250, 128), jnp.float32)
        tbl_7 = 0.05 * jax.random.normal(jax.random.fold_in(_tk, 500 + 7), (12500, 128), jnp.float32)
        tbl_8 = 0.05 * jax.random.normal(jax.random.fold_in(_tk, 500 + 8), (12500, 128), jnp.float32)
        tbl_9 = 0.05 * jax.random.normal(jax.random.fold_in(_tk, 500 + 9), (1000, 128), jnp.float32)
        tbl_10 = 0.05 * jax.random.normal(jax.random.fold_in(_tk, 500 + 10), (12500, 128), jnp.float32)
        tbl_11 = 0.05 * jax.random.normal(jax.random.fold_in(_tk, 500 + 11), (1000, 128), jnp.float32)
        tbl_12 = 0.05 * jax.random.normal(jax.random.fold_in(_tk, 500 + 12), (1250, 128), jnp.float32)
        tbl_13 = 0.05 * jax.random.normal(jax.random.fold_in(_tk, 500 + 13), (1250, 128), jnp.float32)
        tbl_14 = 0.05 * jax.random.normal(jax.random.fold_in(_tk, 500 + 14), (1000, 128), jnp.float32)
        tbl_15 = 0.05 * jax.random.normal(jax.random.fold_in(_tk, 500 + 15), (1250, 128), jnp.float32)
        tbl_16 = 0.05 * jax.random.normal(jax.random.fold_in(_tk, 500 + 16), (12500, 128), jnp.float32)
        tbl_17 = 0.05 * jax.random.normal(jax.random.fold_in(_tk, 500 + 17), (1250, 128), jnp.float32)
        tbl_18 = 0.05 * jax.random.normal(jax.random.fold_in(_tk, 500 + 18), (12500, 128), jnp.float32)
        tbl_19 = 0.05 * jax.random.normal(jax.random.fold_in(_tk, 500 + 19), (12500, 128), jnp.float32)
        tbl_20 = 0.05 * jax.random.normal(jax.random.fold_in(_tk, 500 + 20), (1250, 128), jnp.float32)
        tbl_21 = 0.05 * jax.random.normal(jax.random.fold_in(_tk, 500 + 21), (1000, 128), jnp.float32)
        tbl_22 = 0.05 * jax.random.normal(jax.random.fold_in(_tk, 500 + 22), (1250, 128), jnp.float32)
        tbl_23 = 0.05 * jax.random.normal(jax.random.fold_in(_tk, 500 + 23), (1250, 128), jnp.float32)
        tbl_24 = 0.05 * jax.random.normal(jax.random.fold_in(_tk, 500 + 24), (1000, 128), jnp.float32)
        tbl_25 = 0.05 * jax.random.normal(jax.random.fold_in(_tk, 500 + 25), (12500, 128), jnp.float32)
        tbl_26 = 0.05 * jax.random.normal(jax.random.fold_in(_tk, 500 + 26), (1000, 128), jnp.float32)
        _rk = jax.random.fold_in(_tk, 7)
        W_top1 = 0.0521996 * jax.random.normal(jax.random.fold_in(_tk, 801), (367, 512), jnp.float32)
        W_top2 = 0.0441942 * jax.random.normal(jax.random.fold_in(_tk, 802), (512, 256), jnp.float32)
        W_top3 = 0.0625 * jax.random.normal(jax.random.fold_in(_tk, 803), (256, 1), jnp.float32)
        b_top1 = jnp.zeros((512,), jnp.float32)
        b_top2 = jnp.zeros((256,), jnp.float32)
        return (dense_ctx, ids, tbl_0, tbl_1, tbl_2, tbl_3, tbl_4, tbl_5, tbl_6, tbl_7, tbl_8, tbl_9, tbl_10, tbl_11, tbl_12, tbl_13, tbl_14, tbl_15, tbl_16, tbl_17, tbl_18, tbl_19, tbl_20, tbl_21, tbl_22, tbl_23, tbl_24, tbl_25, tbl_26, W_top1, b_top1, W_top2, b_top2, W_top3)
    dense_ctx, ids, tbl_0, tbl_1, tbl_2, tbl_3, tbl_4, tbl_5, tbl_6, tbl_7, tbl_8, tbl_9, tbl_10, tbl_11, tbl_12, tbl_13, tbl_14, tbl_15, tbl_16, tbl_17, tbl_18, tbl_19, tbl_20, tbl_21, tbl_22, tbl_23, tbl_24, tbl_25, tbl_26, W_top1, b_top1, W_top2, b_top2, W_top3 = _rec_inputs()

    def _L0_rec_setup():
        import jax, jax.numpy as jnp
        import numpy as np
        NUM_FEAS = 27
        key = jax.random.key(seed)
        inputs = jax.random.normal(key, (4096, NUM_FEAS, 128), dtype=jnp.float32)
        return {'inputs': inputs}
    _L0_rec_all = _L0_rec_setup()
    _L0_rec_in = {k: v for k, v in _L0_rec_all.items() if k in ()}
    del _L0_rec_all
    return {'dense_ctx': dense_ctx, 'ids': ids, 'tbl_0': tbl_0, 'tbl_1': tbl_1, 'tbl_2': tbl_2, 'tbl_3': tbl_3, 'tbl_4': tbl_4, 'tbl_5': tbl_5, 'tbl_6': tbl_6, 'tbl_7': tbl_7, 'tbl_8': tbl_8, 'tbl_9': tbl_9, 'tbl_10': tbl_10, 'tbl_11': tbl_11, 'tbl_12': tbl_12, 'tbl_13': tbl_13, 'tbl_14': tbl_14, 'tbl_15': tbl_15, 'tbl_16': tbl_16, 'tbl_17': tbl_17, 'tbl_18': tbl_18, 'tbl_19': tbl_19, 'tbl_20': tbl_20, 'tbl_21': tbl_21, 'tbl_22': tbl_22, 'tbl_23': tbl_23, 'tbl_24': tbl_24, 'tbl_25': tbl_25, 'tbl_26': tbl_26, 'W_top1': W_top1, 'b_top1': b_top1, 'W_top2': W_top2, 'b_top2': b_top2, 'W_top3': W_top3}

def reference(dense_ctx, ids, tbl_0, tbl_1, tbl_2, tbl_3, tbl_4, tbl_5, tbl_6, tbl_7, tbl_8, tbl_9, tbl_10, tbl_11, tbl_12, tbl_13, tbl_14, tbl_15, tbl_16, tbl_17, tbl_18, tbl_19, tbl_20, tbl_21, tbl_22, tbl_23, tbl_24, tbl_25, tbl_26, W_top1, b_top1, W_top2, b_top2, W_top3):
    import jax
    import jax.numpy as jnp

    def _L0_rec_ref(inputs):
        import jax, jax.numpy as jnp
        import numpy as np
        NUM_FEAS = 27
        n = inputs.shape[1]
        dot = jnp.einsum('bnd,bmd->bnm', inputs, inputs)
        iu, ju = jnp.triu_indices(n, k=1)
        return dot[:, iu, ju]
    e = jnp.stack([tbl_0[ids[:, 0]], tbl_1[ids[:, 1]], tbl_2[ids[:, 2]], tbl_3[ids[:, 3]], tbl_4[ids[:, 4]], tbl_5[ids[:, 5]], tbl_6[ids[:, 6]], tbl_7[ids[:, 7]], tbl_8[ids[:, 8]], tbl_9[ids[:, 9]], tbl_10[ids[:, 10]], tbl_11[ids[:, 11]], tbl_12[ids[:, 12]], tbl_13[ids[:, 13]], tbl_14[ids[:, 14]], tbl_15[ids[:, 15]], tbl_16[ids[:, 16]], tbl_17[ids[:, 17]], tbl_18[ids[:, 18]], tbl_19[ids[:, 19]], tbl_20[ids[:, 20]], tbl_21[ids[:, 21]], tbl_22[ids[:, 22]], tbl_23[ids[:, 23]], tbl_24[ids[:, 24]], tbl_25[ids[:, 25]], tbl_26[ids[:, 26]]], axis=1)
    z = _L0_rec_ref(e)
    z = z.reshape(z.shape[0], -1)
    h = jnp.concatenate([z, dense_ctx], axis=1)
    h = jnp.maximum(h @ W_top1 + b_top1, 0.0)
    h = jnp.maximum(h @ W_top2 + b_top2, 0.0)
    y = h @ W_top3
    return y

_drawn_inputs = setup_inputs


def setup_inputs(seed=0):
    import zlib

    import numpy as np

    out = dict(_drawn_inputs(seed))
    spreads = {'b_top1': (0.0, 0.1), 'b_top2': (0.0, 0.1)}
    factors = {}
    for name, (base, spread) in spreads.items():
        noise = np.random.default_rng([zlib.crc32(name.encode()), seed]).standard_normal(out[name].shape)
        drawn = base * np.exp(spread * noise) if base else spread * noise
        out[name] = jnp.asarray(drawn.astype(out[name].dtype))
    for name, factor in factors.items():
        out[name] = (out[name] * factor).astype(out[name].dtype)
    return out
```

```python
import concourse.bass as bass
from concourse import mybir
from contextlib import ExitStack

FP32 = mybir.dt.float32
INT32 = mybir.dt.int32
ALU = mybir.AluOpType
ACT = mybir.ActivationFunctionType

P = 128
B = 512
D = 128
F = 27
FP = 32
NCTX = 16
NPAIR = F * (F - 1) // 2
H1, H2 = 512, 256
CH = B // P
GF = 4
NG = (F + GF - 1) // GF
NS = 4
NQ = P // NS
QB = 4
GB = 4
NBATCH = NQ // (QB * GB)
NL = F - 1
KT = 7
J1, J2 = H1 // P, H2 // P
SLOTS = [range(g, NL, 4) for g in range(4)]
CTX_T, CTX_G = NL // 4, NL % 4
CTX_ROW = 32 * CTX_G


def features_of(group):
    return range(group * GF, min(F, group * GF + GF))


def build(nc, ids, tables, ctx_t, w1, b1, w2, b2, w3, out):
    with ExitStack() as stack:
        def sbuf(name, shape, dt=FP32):
            return stack.enter_context(nc.sbuf_tensor(name, shape, dt))

        def psum(name, shape):
            return stack.enter_context(nc.psum_tensor(name, shape, FP32))

        def sem(name):
            return stack.enter_context(nc.semaphore(name))

        idx = sbuf("idx", [P, CH, F], INT32)
        ident = sbuf("ident", [P, P])
        rows = sbuf("rows", [P, CH, F, D])
        emb = sbuf("emb", [P, CH, NQ, NS, FP])
        z = sbuf("z", [P, KT, B])
        w1s = sbuf("w1s", [P, KT, H1])
        w2s = sbuf("w2s", [P, J1, H2])
        w3s = sbuf("w3s", [P, J2])
        b1s = sbuf("b1s", [P, J1])
        b2s = sbuf("b2s", [P, J2])
        h1 = sbuf("h1", [P, J1, B])
        h2 = sbuf("h2", [P, J2, B])
        y = sbuf("y", [1, B])

        tp = [psum(f"tp{i}", [P, GF, P]) for i in range(2)]
        gram = psum("gram", [P, GB, 512])
        p1 = psum("p1", [P, J1, P])
        p2 = psum("p2", [P, 512])

        ids_in = sem("ids_in")
        gathered = [[sem(f"gathered_{c}_{k}") for k in range(NG)] for c in range(CH)]
        ident_zeroed = sem("ident_zeroed")
        ident_made = sem("ident_made")
        pads_zeroed = sem("pads_zeroed")
        w1_zeroed = sem("w1_zeroed")
        weights_in = sem("weights_in")
        transposed = sem("transposed")
        emb_written = sem("emb_written")
        gram_done = sem("gram_done")
        z_dve = sem("z_dve")
        z_act = sem("z_act")
        l1_done = sem("l1_done")
        h1_written = sem("h1_written")
        l2_done = sem("l2_done")
        h2_written = sem("h2_written")
        l3_done = sem("l3_done")
        y_written = sem("y_written")
        out_stored = sem("out_stored")
        n_weight_dmas = NL + 1 + 5 + 0
        block = stack.enter_context(nc.Block())

        def evict_pairs(copy, half, s):
            c, b = divmod(half, NBATCH)
            src = gram[32 * s:32 * s + 32, :, 0:QB * NS * NL].rearrange(
                "p k (q s n) -> p k q s n", q=QB, s=NS)[:, :, :, s, :]
            nq = QB * GB
            for g in range(4):
                nt = len(SLOTS[g])
                col = c * P + s * NQ + b * nq
                dst = z[32 * g:32 * g + 32, 0:nt, col:col + nq].rearrange("p t (k q) -> p k q t", k=GB)
                last = copy(dst, src[:, :, :, g::4])
            return last

        @block.sync
        def _(sp):
            sp.dma_start(idx[:, :, :], ids.rearrange("(c p) f -> p c f", p=P)).then_inc(ids_in, 16)
            sp.dma_start(z[CTX_ROW:CTX_ROW + NCTX, CTX_T, :], ctx_t).then_inc(weights_in, 16)
            sp.dma_start(w2s[:, :, :], w2.rearrange("(t p) n -> p t n", p=P)).then_inc(weights_in, 16)
            sp.dma_start(w3s[:, :], w3).then_inc(weights_in, 16)
            sp.dma_start(b1s[:, :], b1).then_inc(weights_in, 16)
            sp.dma_start(b2s[:, :], b2).then_inc(weights_in, 16)
            sp.wait_ge(w1_zeroed, 1)
            row = 0
            for n in range(NL):
                t, g = divmod(n, 4)
                cnt = F - 1 - n
                sp.dma_start(w1s[32 * g + n + 1:32 * g + F, t, :], w1[row:row + cnt, :]).then_inc(weights_in, 16)
                row += cnt
            sp.dma_start(w1s[CTX_ROW:CTX_ROW + NCTX, CTX_T, :], w1[NPAIR:NPAIR + NCTX, :]).then_inc(weights_in, 16)
            sp.wait_ge(y_written, CH)
            sp.dma_start(out, y[:, :]).then_inc(out_stored, 16)
            sp.wait_ge(out_stored, 16)

        @block.gpsimd
        def _(pool):
            nc.gpsimd.memset(ident[:, :], 0.0).then_inc(ident_zeroed, 1)
            pool.wait_ge(ident_zeroed, 1)
            nc.gpsimd.affine_select(out=ident[:, :], in_=ident[:, :], compare_op=ALU.not_equal, fill=1.0,
                                    base=0, pattern=[[-1, P]], channel_multiplier=1).then_inc(ident_made, 1)
            pool.wait_ge(ids_in, 16)
            for c in range(CH):
                for k in range(NG):
                    for f in features_of(k):
                        pool.indirect_dma_start(
                            out=rows[:, c, f, :], out_offset=None, in_=tables[f][:, :],
                            in_offset=bass.IndirectOffsetOnAxis(ap=idx[:, c, f:f + 1], axis=0),
                        ).then_inc(gathered[c][k], 16)

        @block.vector
        def _(dve):
            nc.vector.memset(emb[:, :, :, :, F:FP].rearrange("p c q s f -> p (c q s) f"), 0.0).then_inc(pads_zeroed, 1)
            nc.vector.memset(w1s[:, :, :], 0.0).then_inc(w1_zeroed, 1)
            for c in range(CH):
                for k in range(NG):
                    fs = features_of(k)
                    dve.wait_ge(transposed, c * NG + k + 1)
                    nc.vector.tensor_copy(
                        emb[:, c, :, :, fs[0]:fs[-1] + 1],
                        tp[(c * NG + k) % 2][:, 0:len(fs), :].rearrange("p f (s q) -> p q s f", s=NS),
                    ).then_inc(emb_written, 1)
                for b in range(NBATCH):
                    half = c * NBATCH + b
                    dve.wait_ge(gram_done, half + 1)
                    evict_pairs(nc.vector.tensor_copy, half, 0)
                    evict_pairs(nc.vector.tensor_copy, half, 1).then_inc(z_dve, 1)

        @block.scalar
        def _(act):
            for c in range(CH):
                cols = slice(c * P, (c + 1) * P)
                for b in range(NBATCH):
                    half = c * NBATCH + b
                    act.wait_ge(gram_done, half + 1)
                    evict_pairs(nc.scalar.copy, half, 2)
                    evict_pairs(nc.scalar.copy, half, 3).then_inc(z_act, 1)
                if c == 0:
                    act.wait_ge(weights_in, 16 * n_weight_dmas)
                act.wait_ge(l1_done, c + 1)
                for j in range(J1):
                    last = nc.scalar.activation(h1[:, j, cols], p1[:, j, :], ACT.Relu, bias=b1s[:, j:j + 1])
                last.then_inc(h1_written, 1)
                act.wait_ge(l2_done, c + 1)
                for j in range(J2):
                    last = nc.scalar.activation(h2[:, j, cols], p2[:, j * P:(j + 1) * P], ACT.Relu,
                                                bias=b2s[:, j:j + 1])
                last.then_inc(h2_written, 1)
                act.wait_ge(l3_done, c + 1)
                nc.scalar.copy(y[:, cols], p2[0:1, J2 * P:(J2 + 1) * P]).then_inc(y_written, 1)

        @block.tensor
        def _(pe):
            pe.wait_ge(ident_made, 1)
            for c in range(CH):
                cols = slice(c * P, (c + 1) * P)
                for k in range(NG):
                    i = c * NG + k
                    if i >= 2:
                        pe.wait_ge(emb_written, i - 1)
                    fs = features_of(k)
                    pe.wait_ge(gathered[c][k], 16 * len(fs))
                    for f in fs:
                        last = nc.tensor.transpose(tp[i % 2][:, f - fs[0], :], rows[:, c, f, :], ident[:, :])
                    last.then_inc(transposed, 1)
                pe.wait_ge(emb_written, (c + 1) * NG)
                if c == 0:
                    pe.wait_ge(pads_zeroed, 1)
                for b in range(NBATCH):
                    half = c * NBATCH + b
                    if half >= 1:
                        pe.wait_ge(z_dve, half)
                        pe.wait_ge(z_act, half)
                    for k in range(GB):
                        for qq in range(QB):
                            q = (b * GB + k) * QB + qq
                            last = nc.tensor.matmul(
                                gram[:, k, qq * NS * NL:(qq + 1) * NS * NL],
                                emb[:, c, q, :, :].rearrange("p s f -> p (s f)"), emb[:, c, q, :, 0:NL], start=True, stop=True)
                    last.then_inc(gram_done, 1)
                pe.wait_ge(z_dve, (c + 1) * NBATCH)
                pe.wait_ge(z_act, (c + 1) * NBATCH)
                if c == 0:
                    pe.wait_ge(weights_in, 16 * n_weight_dmas)
                for j in range(J1):
                    for t in range(KT):
                        k = P if t < KT - 1 else CTX_ROW + NCTX
                        last = nc.tensor.matmul(p1[:, j, :], w1s[0:k, t, j * P:(j + 1) * P], z[0:k, t, cols],
                                                start=(t == 0), stop=(t == KT - 1))
                last.then_inc(l1_done, 1)
                pe.wait_ge(h1_written, c + 1)
                if c >= 1:
                    pe.wait_ge(y_written, c)
                for j in range(J2):
                    for t in range(J1):
                        last = nc.tensor.matmul(p2[:, j * P:(j + 1) * P], w2s[:, t, j * P:(j + 1) * P], h1[:, t, cols],
                                                start=(t == 0), stop=(t == J1 - 1))
                last.then_inc(l2_done, 1)
                pe.wait_ge(h2_written, c + 1)
                for t in range(J2):
                    last = nc.tensor.matmul(p2[0:1, J2 * P:(J2 + 1) * P], w3s[:, t:t + 1], h2[:, t, cols],
                                            start=(t == 0), stop=(t == J2 - 1))
                last.then_inc(l3_done, 1)


def kernel(**inputs):
    import numpy as _np
    import concourse.bacc as _bacc
    from concourse import mybir as _mybir
    from concourse.bass_utils import run_bass_kernel_spmd as _run

    nc = _bacc.Bacc("TRN2", target_bir_lowering=False, num_devices=1)
    arrays = {}

    def dram(name, a):
        a = _np.ascontiguousarray(a)
        arrays[f"in_{name}_dram"] = a
        return nc.dram_tensor(f"in_{name}_dram", a.shape, _mybir.dt.from_np(a.dtype), kind="ExternalInput").ap()

    ids = dram("ids", inputs["ids"])
    tables = [dram(f"tbl_{f}", inputs[f"tbl_{f}"]) for f in range(F)]
    ctx_t = dram("ctx_t", _np.asarray(inputs["dense_ctx"]).T)
    w1 = dram("W_top1", inputs["W_top1"])
    b1 = dram("b_top1", _np.asarray(inputs["b_top1"]).reshape(J1, P).T)
    w2 = dram("W_top2", inputs["W_top2"])
    b2 = dram("b_top2", _np.asarray(inputs["b_top2"]).reshape(J2, P).T)
    w3 = dram("W_top3", _np.asarray(inputs["W_top3"]).reshape(J2, P).T)
    out = nc.dram_tensor("out_0_dram", (1, B), FP32, kind="ExternalOutput").ap()
    build(nc, ids, tables, ctx_t, w1, b1, w2, b2, w3, out)
    r = _run(nc, [arrays], core_ids=[0])
    return _np.asarray(r.results[0]["out_0_dram"]).reshape(B, 1)
```

```python
import concourse.bass as bass
from concourse import mybir
from contextlib import ExitStack

FP32 = mybir.dt.float32
FP32R = mybir.dt.float32r
INT32 = mybir.dt.int32
ALU = mybir.AluOpType
ACT = mybir.ActivationFunctionType

P = 128
B = 512
D = 128
F = 27
FP = 32
NCTX = 16
NPAIR = F * (F - 1) // 2
H1, H2 = 512, 256
J1, J2 = H1 // P, H2 // P
NL = F - 1
CH = B // P
NS = 4
NQ = P // NS
GB = 2
GF = 4

N_PICK = 7
PICK_LOW = 3
SPLIT = 15
TABLE_ROWS = 1250
IDS_PARTS = [(0, 1), (1, 3), (3, N_PICK)]
RING = 14
SPLITS = 3
ROW_CHUNKS = 3
ACT_HOT = 2

KT = 3
LOW = range(1, SPLIT)
HIGH = range(SPLIT, F)
LOW_STEPS = (len(LOW) + 3) // 4
HIGH_ROWS = [SPLIT + KT * g + KT - 1 for g in range(4)]


def high_place(n):
    return divmod(n - SPLIT, KT)


def low_place(n):
    return (n - 1) % 4, (n - 1) // 4


def pack_free_rows():
    free = [[32 - HIGH_ROWS[g], 32 * g + HIGH_ROWS[g], t] for g in range(4) for t in range(KT)]
    slots = {}
    for n in reversed(LOW):
        room = min((f for f in free if f[0] >= n), key=lambda f: f[0])
        slots[n] = (room[1], room[2])
        room[0] -= n
        room[1] += n
    ctx, row = [], 0
    for room in sorted(free, key=lambda f: -f[0]):
        k = min(room[0], NCTX - row)
        if k > 0:
            ctx.append((row, k, room[1], room[2]))
            row += k
    return slots, ctx


LOW_AT, CTX_AT = pack_free_rows()


def plan_features(rows):
    order = sorted(range(F), key=lambda f: (rows[f], f))
    picked, gathered = sorted(order[:N_PICK]), sorted(order[N_PICK:])
    n_low = SPLIT - PICK_LOW
    return picked[:PICK_LOW] + gathered[:n_low] + gathered[n_low:] + picked[PICK_LOW:]


PICK_POS = list(range(PICK_LOW)) + list(range(F - N_PICK + PICK_LOW, F))
GATHER_POS = range(PICK_LOW, F - N_PICK + PICK_LOW)
LOW_GROUPS = [range(a, min(a + GF, SPLIT)) for a in range(PICK_LOW, SPLIT, GF)]
GROUPS = LOW_GROUPS + [range(a, min(a + GF, GATHER_POS[-1] + 1)) for a in range(SPLIT, GATHER_POS[-1] + 1, GF)]


MOVED = CH - 2
LOW_GROUPS_N = len(LOW_GROUPS)


class GramStep:

    def __init__(self, chunk, q0, nq, n0=1, n1=F):
        self.chunk, self.q0, self.nq, self.n0, self.n1 = chunk, q0, nq, n0, n1
        self.per_bank = nq // GB
        self.width = NS * (n1 - n0)
        self.m = 32 * (NS - 1) + n1 - 1
        assert self.per_bank * self.width <= 512


GRAMS_OF_CHUNK = 4
GRAMS = [GramStep(c, q0, NQ // GRAMS_OF_CHUNK) for c in range(CH) for q0 in range(0, NQ, NQ // GRAMS_OF_CHUNK)]


def turns(chunk, first=0, end=len(GROUPS)):
    return [("turn", chunk, k) for k in range(first, end)]


def grams(chunk, first=0, end=GRAMS_OF_CHUNK):
    return [("gram", chunk * GRAMS_OF_CHUNK + i) for i in range(first, end)]


def weave(*runs):
    return [step for run in runs for step in run]


def picks(first, end):
    return [("pick", i) for i in range(first, end)]


STEPS = weave(
    picks(0, 4), turns(0, 0, 1), picks(4, 5), turns(0, 1, 3), picks(5, 6), turns(0, 3, 4), picks(6, 7), turns(0, 4),
    picks(7, N_PICK),
    grams(0, 0, 2), turns(1, 0, 1), grams(0, 2, 3), turns(1, 1, 3), grams(0, 3, 4), turns(1, 3),
    grams(1), turns(2, 0, 2), [("layer1", 0)], turns(2, 2, 3), [("layer2", 0)], turns(2, 3, 4), [("layer3", 0)],
    turns(2, 4), grams(2, 0, 2), [("layer1", 1)], grams(2, 2, 3), [("layer2", 1)], grams(2, 3), [("layer3", 1)],
    turns(3, 0, 2), [("layer1", 2)], turns(3, 2, 3), [("layer2", 2)], turns(3, 3, 4), [("layer3", 2)], turns(3, 4),
    grams(3), [("layer1", 3), ("layer2", 3), ("layer3", 3)])

FILLS = [s for s in STEPS if s[0] in ("pick", "turn")]


def on_act(step):
    return step[0] == "pick" or step[2] % 2 == 1


def evicted(step):
    return sum(1 for s in FILLS[:FILLS.index(step) + 1] if on_act(s) == on_act(step))


def turned_at(step):
    return sum(1 for s in FILLS[:FILLS.index(step) + 1] if s[0] == "turn")


def build(nc, ids, ids_t, tables, feature, ctx_t, w1, w1_low, b1, w2, b2, w3, out):
    with ExitStack() as stack:
        def sbuf(name, shape, dt=FP32):
            return stack.enter_context(nc.sbuf_tensor(name, shape, dt))

        def psum(name, shape):
            return stack.enter_context(nc.psum_tensor(name, shape, FP32))

        def sem(name):
            return stack.enter_context(nc.semaphore(name))

        picked = [tables[feature[pos]] for pos in PICK_POS]
        blocks = [-(-t.shape[0] // P) for t in picked]
        parts = [t.shape[0] // b for t, b in zip(picked, blocks)]
        assert all(p * b == t.shape[0] for p, b, t in zip(parts, blocks, picked))
        first_block = [sum(blocks[:i]) for i in range(N_PICK + 1)]
        max_blocks = max(blocks)
        spread = P - 16

        idx = sbuf("idx", [P, CH, F], INT32)
        ids_all = sbuf("ids_all", [P, N_PICK, B], INT32)
        row_of = {b: sbuf(f"row_of_{b}", [P, b]) for b in sorted(set(blocks))}
        minus_row = {b: sbuf(f"minus_row_{b}", [P, b]) for b in sorted(set(blocks))}
        table = sbuf("table", [P, 2, max_blocks, D])
        table_hi = sbuf("table_hi", [P, SPLITS, max_blocks, D], FP32R)
        table_lo = sbuf("table_lo", [P, SPLITS, max_blocks, D], FP32R)
        hot = sbuf("hot", [P, RING, B], FP32R)
        distance = sbuf("distance", [P, ACT_HOT, B])
        ident = sbuf("ident", [P, P])
        rows = sbuf("rows", [P, ROW_CHUNKS, len(GATHER_POS), D])
        emb = sbuf("emb", [P, CH, NQ, NS, FP])
        z = sbuf("z", [P, KT, B])
        z_low = sbuf("z_low", [P, LOW_STEPS, B])
        w1s = sbuf("w1s", [P, KT, H1])
        w2s = sbuf("w2s", [P, J1, H2])
        w3s = sbuf("w3s", [P, J2])
        b1s = sbuf("b1s", [P, J1])
        b2s = sbuf("b2s", [P, J2])
        h1 = sbuf("h1", [P, 2, J1, P])
        h2 = sbuf("h2", [P, 2, J2, P])
        y = sbuf("y", [1, B])

        turn_bank = [psum(f"turn_bank_{i}", [P, GF, P]) for i in range(2)]
        gram = psum("gram", [P, 2 * GB, 512])
        hidden = [psum(f"hidden_{i}", [P, 4, P]) for i in range(2)]

        low_w1 = table[:, :, :, :].rearrange("p a b d -> p (a b d)")[:, 0:LOW_STEPS * H1]
        ids_in = sem("ids_in")
        ids_all_in = [sem(f"ids_all_in_{part}") for part in range(len(IDS_PARTS))]
        table_in = [sem(f"table_in_{i}") for i in range(2)]
        gathered = [[sem(f"gathered_{c}_{k}") for k in range(len(GROUPS))] for c in range(CH)]
        rows_numbered = sem("rows_numbered")
        rows_negated = sem("rows_negated")
        ident_zeroed = sem("ident_zeroed")
        ident_made = sem("ident_made")
        emb_zeroed = sem("emb_zeroed")
        z_zeroed = sem("z_zeroed")
        hi_written = sem("hi_written")
        lo_written = sem("lo_written")
        hot_dve = sem("hot_dve")
        hot_act = sem("hot_act")
        distance_written = sem("distance_written")
        hot_used = sem("hot_used")
        weights_in = sem("weights_in")
        turned = sem("turned")
        emb_act = sem("emb_act")
        emb_dve = sem("emb_dve")
        gram_done = sem("gram_done")
        z_dve = sem("z_dve")
        z_act = sem("z_act")
        low_moved = [sem(f"low_moved_{c}") for c in range(MOVED)]
        low_w1_in = sem("low_w1_in")
        l1_done = sem("l1_done")
        h1_written = sem("h1_written")
        l2_done = sem("l2_done")
        h2_written = sem("h2_written")
        l3_done = sem("l3_done")
        y_written = sem("y_written")
        out_stored = sem("out_stored")
        n_weight_dmas = 5 + len(CTX_AT)
        block = stack.enter_context(nc.Block())

        def ids_part(i):
            return next(k for k, (a, e) in enumerate(IDS_PARTS) if a <= i < e)

        def act_blocks(i):
            return range(blocks[i] - ACT_HOT, blocks[i])

        def hot_slot(i, k):
            return (first_block[i] + k) % RING

        def low_evicted(c):
            return 1 + max(i for i, g in enumerate(GRAMS) if g.chunk == c and g.n0 < SPLIT)

        def evict_turn(engine, copy, step):
            _, c, k = step
            group = GROUPS[k]
            engine.wait_ge(turned, turned_at(step))
            return copy(emb[:, c, :, :, group[0]:group[-1] + 1],
                        turn_bank[FILLS.index(step) % 2][:, 0:len(group), :].rearrange("p f (s q) -> p q s f", s=NS))

        def evict_gram(copy, i, quadrants):
            step = GRAMS[i]
            n, bank, col = step.per_bank, (i % 2) * GB, step.chunk * P + step.q0
            for s in quadrants:
                src = gram[32 * s:32 * s + 32, bank:bank + GB, 0:n * step.width].rearrange(
                    "p k (q s n) -> p k q s n", q=n, s=NS)[:, :, :, s, :]
                cols = slice(col + s * NQ, col + s * NQ + step.nq)
                for g in range(4):
                    if step.n0 < SPLIT:
                        first, steps = 1 + g - step.n0, len(range(1 + g, SPLIT, 4))
                        dst = z_low[32 * g:32 * g + SPLIT - 1, 0:steps, cols]
                        last = copy(dst.rearrange("p t (k q) -> p k q t", k=GB),
                                    src[0:SPLIT - 1, :, :, first:first + 4 * steps - 3:4])
                    if step.n1 > SPLIT:
                        first = SPLIT + KT * g - step.n0
                        dst = z[32 * g:32 * g + HIGH_ROWS[g], :, cols]
                        last = copy(dst.rearrange("p t (k q) -> p k q t", k=GB),
                                    src[0:HIGH_ROWS[g], :, :, first:first + KT])
            return last

        @block.sync
        def _(sp):
            def load_table(i):
                if i >= 2:
                    sp.wait_ge(lo_written, i - 1)
                view = picked[i].rearrange("(p b) d -> p b d", b=blocks[i])
                for a, e in ((0, spread), (spread, parts[i])):
                    sp.dma_start(table[a:e, i % 2, 0:blocks[i], :], view[a:e, :, :]).then_inc(table_in[i % 2], 16)

            def load_ids(part):
                a, e = IDS_PARTS[part]
                sp.dma_start(ids_all[:, a:e, :].rearrange("p i b -> p (i b)"),
                             ids_t[0:1, a * B:e * B].to_broadcast([P, (e - a) * B])).then_inc(ids_all_in[part], 16)

            sp.dma_start(idx[:, :, :], ids.rearrange("(c p) f -> p c f", p=P)).then_inc(ids_in, 16)
            load_ids(0)
            load_table(0)
            load_ids(1)
            load_table(1)
            load_ids(2)
            for i in range(2, N_PICK):
                load_table(i)
            sp.dma_start(w1s[:, :, :], w1).then_inc(weights_in, 16)
            sp.dma_start(w2s[:, :, :], w2.rearrange("(t p) n -> p t n", p=P)).then_inc(weights_in, 16)
            sp.dma_start(w3s[:, :], w3).then_inc(weights_in, 16)
            sp.dma_start(b1s[:, :], b1).then_inc(weights_in, 16)
            sp.dma_start(b2s[:, :], b2).then_inc(weights_in, 16)
            sp.wait_ge(z_zeroed, 2)
            for row, k, part, t in CTX_AT:
                sp.dma_start(z[part:part + k, t, :], ctx_t[row:row + k, :]).then_inc(weights_in, 16)
            sp.wait_ge(lo_written, N_PICK)
            sp.dma_start(low_w1, w1_low).then_inc(low_w1_in, 16)
            for c in range(MOVED):
                sp.wait_ge(z_dve, low_evicted(c))
                sp.wait_ge(z_act, low_evicted(c))
                cols = slice(c * P, (c + 1) * P)
                for n in LOW:
                    g, t = low_place(n)
                    part, kt = LOW_AT[n]
                    sp.dma_start(z[part:part + n, kt, cols], z_low[32 * g:32 * g + n, t, cols]).then_inc(
                        low_moved[c], 16)
            sp.wait_ge(y_written, CH)
            sp.dma_start(out, y[:, :]).then_inc(out_stored, 16)
            sp.wait_ge(out_stored, 16)

        @block.gpsimd
        def _(pool):
            for b in row_of:
                nc.gpsimd.iota(row_of[b][:, :], pattern=[[1, b]], base=0, channel_multiplier=b,
                               allow_small_or_imprecise_dtypes=True).then_inc(rows_numbered, 1)
            nc.gpsimd.memset(ident[:, :], 0.0).then_inc(ident_zeroed, 1)
            pool.wait_ge(ident_zeroed, 1)
            nc.gpsimd.affine_select(out=ident[:, :], in_=ident[:, :], compare_op=ALU.not_equal, fill=1.0,
                                    base=0, pattern=[[-1, P]], channel_multiplier=1).then_inc(ident_made, 1)
            nc.gpsimd.memset(z[:, :, :], 0.0).then_inc(z_zeroed, 1)
            nc.gpsimd.memset(z_low[:, :, MOVED * P:B], 0.0).then_inc(z_zeroed, 1)
            pool.wait_ge(ids_in, 16)
            for c in range(CH):
                for k, group in enumerate(GROUPS):
                    if c >= ROW_CHUNKS:
                        pool.wait_ge(turned, turned_at(("turn", c - ROW_CHUNKS, k)))
                    for pos in group:
                        f = feature[pos]
                        pool.indirect_dma_start(
                            out=rows[:, c % ROW_CHUNKS, pos - PICK_LOW, :], out_offset=None, in_=tables[f][:, :],
                            in_offset=bass.IndirectOffsetOnAxis(ap=idx[:, c, f:f + 1], axis=0),
                        ).then_inc(gathered[c][k], 16)

        @block.vector
        def _(dve):
            def make_hot(i):
                dve.wait_ge(ids_all_in[ids_part(i)], 16)
                n = parts[i]
                for k in range(blocks[i]):
                    if k in act_blocks(i):
                        continue
                    if first_block[i] + k >= RING:
                        dve.wait_ge(hot_used, first_block[i] + k - RING + 1)
                    nc.vector.tensor_scalar(hot[0:n, hot_slot(i, k), :], ids_all[0:n, i, :],
                                            row_of[blocks[i]][0:n, k:k + 1], None, ALU.is_equal).then_inc(hot_dve, 1)

            def split_low(i):
                n = parts[i]
                dve.wait_ge(hi_written, i + 1)
                if i >= SPLITS:
                    dve.wait_ge(hot_used, first_block[i - SPLITS + 1])
                nc.vector.tensor_tensor(table_lo[0:n, i % SPLITS, 0:blocks[i], :], table[0:n, i % 2, 0:blocks[i], :],
                                        table_hi[0:n, i % SPLITS, 0:blocks[i], :].bitcast(FP32),
                                        ALU.subtract).then_inc(lo_written, 1)

            nc.vector.memset(emb[:, :, :, :, F:FP].rearrange("p c q s f -> p (c q s) f"), 0.0).then_inc(emb_zeroed, 1)
            dve.wait_ge(rows_numbered, len(row_of))
            make_hot(0)
            split_low(0)
            split_low(1)
            for step in STEPS:
                if step[0] == "pick":
                    i = step[1]
                    if i + 1 < N_PICK:
                        make_hot(i + 1)
                    if i + 2 < N_PICK:
                        split_low(i + 2)
                elif step[0] == "turn" and not on_act(step):
                    evict_turn(dve, nc.vector.tensor_copy, step).then_inc(emb_dve, 1)
                elif step[0] == "gram":
                    if step[1] == 0:
                        dve.wait_ge(z_zeroed, 2)
                    dve.wait_ge(gram_done, step[1] + 1)
                    evict_gram(nc.vector.tensor_copy, step[1], (0, 1)).then_inc(z_dve, 1)

        @block.scalar
        def _(act):
            def split_high(i):
                n = parts[i]
                act.wait_ge(table_in[i % 2], 32 * (i // 2 + 1))
                if i >= SPLITS:
                    act.wait_ge(hot_used, first_block[i - SPLITS + 1])
                nc.scalar.copy(table_hi[0:n, i % SPLITS, 0:blocks[i], :], table[0:n, i % 2, 0:blocks[i], :]).then_inc(
                    hi_written, 1)

            def make_hot(i):
                n = parts[i]
                act.wait_ge(ids_all_in[ids_part(i)], 16)
                for d, k in enumerate(act_blocks(i)):
                    if i >= 1:
                        act.wait_ge(hot_act, ACT_HOT * (i - 1) + d + 1)
                    nc.scalar.activation(distance[0:n, d, :], ids_all[0:n, i, :], ACT.Abs,
                                         bias=minus_row[blocks[i]][0:n, k:k + 1]).then_inc(distance_written, 1)
                for d, k in enumerate(act_blocks(i)):
                    if first_block[i] + k >= RING:
                        act.wait_ge(hot_used, first_block[i] + k - RING + 1)
                    act.wait_ge(distance_written, ACT_HOT * i + d + 1)
                    nc.scalar.activation(hot[0:n, hot_slot(i, k), :], distance[0:n, d, :], ACT.Relu,
                                         bias=1.0, scale=-1.0).then_inc(hot_act, 1)

            act.wait_ge(rows_numbered, len(row_of))
            for b in row_of:
                nc.scalar.mul(minus_row[b][:, :], row_of[b][:, :], -1.0).then_inc(rows_negated, 1)
            split_high(0)
            act.wait_ge(rows_negated, len(row_of))
            make_hot(0)
            split_high(1)
            for step in STEPS:
                if step[0] == "pick":
                    i = step[1]
                    fill = FILLS.index(step)
                    if i + 1 < N_PICK:
                        make_hot(i + 1)
                    act.wait_ge(hot_used, first_block[i + 1])
                    nc.scalar.copy(
                        emb[:, :, :, :, PICK_POS[i]],
                        turn_bank[fill % 2][:, :, :].rearrange("p c (s q) -> p c q s", s=NS)).then_inc(emb_act, 1)
                    if i + 2 < N_PICK:
                        split_high(i + 2)
                elif step[0] == "turn" and on_act(step):
                    evict_turn(act, nc.scalar.copy, step).then_inc(emb_act, 1)
                elif step[0] == "gram":
                    if step[1] == 0:
                        act.wait_ge(z_zeroed, 2)
                    act.wait_ge(gram_done, step[1] + 1)
                    evict_gram(nc.scalar.copy, step[1], (2, 3)).then_inc(z_act, 1)
                elif step[0] == "layer1":
                    c = step[1]
                    if c == 0:
                        act.wait_ge(weights_in, 16 * n_weight_dmas)
                    for j in range(J1):
                        if j % 2 == 0:
                            act.wait_ge(l1_done, 2 * c + j // 2 + 1)
                        last = nc.scalar.activation(h1[:, c % 2, j, :], hidden[j // 2][:, j % 2, :], ACT.Relu,
                                                    bias=b1s[:, j:j + 1])
                    last.then_inc(h1_written, 1)
                elif step[0] == "layer2":
                    c = step[1]
                    for j in range(J2):
                        act.wait_ge(l2_done, 2 * c + j + 1)
                        last = nc.scalar.activation(h2[:, c % 2, j, :], hidden[j][:, 2, :], ACT.Relu,
                                                    bias=b2s[:, j:j + 1])
                    last.then_inc(h2_written, 1)
                elif step[0] == "layer3":
                    c = step[1]
                    act.wait_ge(l3_done, c + 1)
                    nc.scalar.copy(y[:, c * P:(c + 1) * P], hidden[0][0:1, 3, :]).then_inc(y_written, 1)

        @block.tensor
        def _(pe):
            def wait_bank(fill):
                if fill >= 2:
                    before = FILLS[fill - 2]
                    pe.wait_ge(emb_act if on_act(before) else emb_dve, evicted(before))

            pe.wait_ge(ident_made, 1)
            for step in STEPS:
                if step[0] == "pick":
                    i = step[1]
                    fill = FILLS.index(step)
                    wait_bank(fill)
                    pe.wait_ge(hi_written, i + 1)
                    n = parts[i]
                    bank = turn_bank[fill % 2][:, :, :].rearrange("p c s -> p (c s)")
                    dve_blocks = blocks[i] - ACT_HOT
                    for k in range(blocks[i]):
                        if k in act_blocks(i):
                            pe.wait_ge(hot_act, ACT_HOT * i + k - dve_blocks + 1)
                        else:
                            pe.wait_ge(hot_dve, first_block[i] - ACT_HOT * i + k + 1)
                        nc.tensor.matmul(bank, table_hi[0:n, i % SPLITS, k, :], hot[0:n, hot_slot(i, k), :],
                                         start=(k == 0), stop=False)
                    pe.wait_ge(lo_written, i + 1)
                    for k in range(blocks[i]):
                        last = nc.tensor.matmul(bank, table_lo[0:n, i % SPLITS, k, :], hot[0:n, hot_slot(i, k), :],
                                                start=False, stop=(k == blocks[i] - 1))
                        last.then_inc(hot_used, 1)
                elif step[0] == "turn":
                    _, c, k = step
                    group = GROUPS[k]
                    fill = FILLS.index(step)
                    wait_bank(fill)
                    pe.wait_ge(gathered[c][k], 16 * len(group))
                    for pos in group:
                        last = nc.tensor.transpose(turn_bank[fill % 2][:, pos - group[0], :],
                                                   rows[:, c % ROW_CHUNKS, pos - PICK_LOW, :], ident[:, :])
                    last.then_inc(turned, 1)
                elif step[0] == "gram":
                    i = step[1]
                    g = GRAMS[i]
                    if i == 0:
                        pe.wait_ge(emb_zeroed, 1)
                    if i >= 2:
                        pe.wait_ge(z_dve, i - 1)
                        pe.wait_ge(z_act, i - 1)
                    if g.q0 == 0:
                        own = [s for s in FILLS if s[0] == "pick" or (s[1] == g.chunk and GROUPS[s[2]][0] < g.n1)]
                        pe.wait_ge(emb_act, max(evicted(s) for s in own if on_act(s)))
                        pe.wait_ge(emb_dve, max(evicted(s) for s in own if not on_act(s)))
                    for k in range(GB):
                        for qq in range(g.per_bank):
                            q = g.q0 + k * g.per_bank + qq
                            last = nc.tensor.matmul(
                                gram[0:g.m, (i % 2) * GB + k, qq * g.width:(qq + 1) * g.width],
                                emb[:, g.chunk, q, :, :].rearrange("p s f -> p (s f)")[:, 0:g.m],
                                emb[:, g.chunk, q, :, g.n0:g.n1], start=True, stop=True)
                    last.then_inc(gram_done, 1)
                elif step[0] == "layer1":
                    c = step[1]
                    cols = slice(c * P, (c + 1) * P)
                    if c == 0:
                        pe.wait_ge(weights_in, 16 * n_weight_dmas)
                    else:
                        pe.wait_ge(y_written, c)
                    pe.wait_ge(z_dve, GRAMS_OF_CHUNK * (c + 1))
                    pe.wait_ge(z_act, GRAMS_OF_CHUNK * (c + 1))
                    terms = [(w1s[:, t, :], z[:, t, cols]) for t in range(KT)]
                    if c < MOVED:
                        pe.wait_ge(low_moved[c], 16 * len(LOW))
                    else:
                        pe.wait_ge(low_w1_in, 16)
                        terms += [(low_w1[:, t * H1:(t + 1) * H1], z_low[:, t, cols]) for t in range(LOW_STEPS)]
                    for j in range(J1):
                        for t, (w, x) in enumerate(terms):
                            last = nc.tensor.matmul(hidden[j // 2][:, j % 2, :], w[:, j * P:(j + 1) * P], x,
                                                    start=(t == 0), stop=(t == len(terms) - 1))
                        if j % 2 == 1:
                            last.then_inc(l1_done, 1)
                elif step[0] == "layer2":
                    c = step[1]
                    pe.wait_ge(h1_written, c + 1)
                    for j in range(J2):
                        for t in range(J1):
                            last = nc.tensor.matmul(hidden[j][:, 2, :], w2s[:, t, j * P:(j + 1) * P],
                                                    h1[:, c % 2, t, :], start=(t == 0), stop=(t == J1 - 1))
                        last.then_inc(l2_done, 1)
                elif step[0] == "layer3":
                    c = step[1]
                    pe.wait_ge(h2_written, c + 1)
                    for t in range(J2):
                        last = nc.tensor.matmul(hidden[0][0:1, 3, :], w3s[:, t:t + 1],
                                                h2[:, c % 2, t, :], start=(t == 0), stop=(t == J2 - 1))
                    last.then_inc(l3_done, 1)


def kernel(**inputs):
    import numpy as _np
    import concourse.bacc as _bacc
    from concourse import mybir as _mybir
    from concourse.bass_utils import run_bass_kernel_spmd as _run

    nc = _bacc.Bacc("TRN2", target_bir_lowering=False, num_devices=1)
    arrays = {}

    def dram(name, a):
        a = _np.ascontiguousarray(a)
        arrays[f"in_{name}_dram"] = a
        return nc.dram_tensor(f"in_{name}_dram", a.shape, _mybir.dt.from_np(a.dtype), kind="ExternalInput").ap()

    ids = dram("ids", inputs["ids"])
    tables = [dram(f"tbl_{f}", inputs[f"tbl_{f}"]) for f in range(F)]
    feature = plan_features([t.shape[0] for t in tables])
    ids_t = dram("ids_t", _np.asarray(inputs["ids"]).T[[feature[pos] for pos in PICK_POS]].reshape(1, N_PICK * B))
    ctx_t = dram("ctx_t", _np.asarray(inputs["dense_ctx"]).T)
    w_top1 = _np.asarray(inputs["W_top1"])
    w1_rows = _np.zeros((P, KT, H1), w_top1.dtype)
    first_pair = [f * (F - 1) - f * (f - 1) // 2 - f - 1 for f in range(F)]
    w1_low_rows = _np.zeros((P, LOW_STEPS, H1), w_top1.dtype)
    for n in range(1, F):
        part, t = LOW_AT[n] if n < SPLIT else (32 * high_place(n)[0], high_place(n)[1])
        for m in range(n):
            a, b = sorted((feature[m], feature[n]))
            w1_rows[part + m, t] = w_top1[first_pair[a] + b]
            if n < SPLIT:
                g, t_low = low_place(n)
                w1_low_rows[32 * g + m, t_low] = w_top1[first_pair[a] + b]
    w1_low = dram("W_top1_low", w1_low_rows.reshape(P, LOW_STEPS * H1))
    for row, k, part, t in CTX_AT:
        w1_rows[part:part + k, t] = w_top1[NPAIR + row:NPAIR + row + k]
    w1 = dram("W_top1", w1_rows)
    b1 = dram("b_top1", _np.asarray(inputs["b_top1"]).reshape(J1, P).T)
    w2 = dram("W_top2", inputs["W_top2"])
    b2 = dram("b_top2", _np.asarray(inputs["b_top2"]).reshape(J2, P).T)
    w3 = dram("W_top3", _np.asarray(inputs["W_top3"]).reshape(J2, P).T)
    out = nc.dram_tensor("out_0_dram", (1, B), FP32, kind="ExternalOutput").ap()
    build(nc, ids, ids_t, tables, feature, ctx_t, w1, w1_low, b1, w2, b2, w3, out)
    r = _run(nc, [arrays], core_ids=[0])
    return _np.asarray(r.results[0]["out_0_dram"]).reshape(B, 1)
```

```python
import concourse.bass as bass
from concourse import mybir
from contextlib import ExitStack

FP32 = mybir.dt.float32
FP32R = mybir.dt.float32r
INT32 = mybir.dt.int32
ALU = mybir.AluOpType
ACT = mybir.ActivationFunctionType

P = 128
B = 512
D = 128
F = 27
FP = 32
NCTX = 16
NPAIR = F * (F - 1) // 2
H1, H2 = 512, 256
J1, J2 = H1 // P, H2 // P
CH = B // P
NS = 4
NQ = P // NS
GB = 2
GF = 4

N_PICK = 8
IDS_PARTS = [(0, 1), (1, 2), (2, 3), (3, 5), (5, N_PICK)]
TABLES = 3
RING = 15
SPLITS = 3
ROW_CHUNKS = 3
LEAD = 2
ACT_HOT = 2

KT = 4
REPEATED = range(3, 6)
SLOTS = [
    (9, range(0, 8, 2), range(19, 23)),
    (10, range(7, 11), range(23, 27)),
    (19, range(12, 20, 2), range(0, 4)),
    (16, range(11, 19, 2), range(6, 10))]
ROWS = [F + len(REPEATED)] * 3 + [F]
FR = ROWS[0]
M_GRAM = 32 * (NS - 1) + FR


def position(row):
    return row if row < F else REPEATED[row - F]


def pair_places():
    places = {}
    for g, (split, left, right) in enumerate(SLOTS):
        for t in range(KT):
            for row in range(ROWS[g]):
                m, n = position(row), (left if row < split else right)[t]
                if m != n:
                    places.setdefault((min(m, n), max(m, n)), (32 * g + row, t))
    assert len(places) == NPAIR
    return places


PAIR_AT = pair_places()
CTX_ROWS = 32 - ROWS[3]
CTX_AT = [(row, min(CTX_ROWS, NCTX - row), 96 + ROWS[3], row // CTX_ROWS) for row in range(0, NCTX, CTX_ROWS)]


def plan_features(rows):
    order = sorted(range(F), key=lambda f: (rows[f], f))
    return sorted(order[:N_PICK]) + sorted(order[N_PICK:])


GATHER_POS = range(N_PICK, F)
GROUPS = [range(a, min(a + GF, F - 1)) for a in range(N_PICK, F - 1, GF)] + [range(F - 1, F)]
GRAMS_OF_CHUNK = 4
STEP_Q = NQ // GRAMS_OF_CHUNK
BANK_Q = STEP_Q // GB
BANK_COLS = BANK_Q * NS * F
assert BANK_COLS <= 512


def turns(chunk, first=0, end=len(GROUPS)):
    return [("turn", chunk, k) for k in range(first, end)]


def grams(chunk, first=0, end=GRAMS_OF_CHUNK):
    return [("gram", chunk * GRAMS_OF_CHUNK + i) for i in range(first, end)]


def layer(n, chunk):
    return [(f"layer{n}", chunk)]


def weave(*runs):
    return [step for run in runs for step in run]


def picks(first, end):
    return [("pick", i) for i in range(first, end)]


STEPS = weave(
    picks(0, 4), turns(0, 0, 2), picks(4, 5), turns(0, 2, 3), picks(5, 6), turns(0, 3, 4), picks(6, 7), turns(0, 4),
    picks(7, N_PICK), turns(1, 0, 2),
    grams(0, 0, 1), turns(1, 2, 3), grams(0, 1, 2), turns(1, 3, 4), grams(0, 2, 3), turns(1, 4), grams(0, 3),
    grams(1, 0, 3), turns(2, 0, 1), grams(1, 3), layer(1, 0), turns(2, 1, 2), layer(2, 0), turns(2, 2, 3), layer(3, 0),
    turns(2, 3, 4), layer(1, 1), turns(2, 4), layer(2, 1),
    grams(2, 0, 2), turns(3, 0, 1), grams(2, 2, 3), layer(3, 1), grams(2, 3), turns(3, 1, 3),
    layer(1, 2), turns(3, 3, 4), layer(2, 2), turns(3, 4), layer(3, 2),
    grams(3), layer(1, 3), layer(2, 3), layer(3, 3))

FILLS = [s for s in STEPS if s[0] in ("pick", "turn")]

EARLY = sum(1 for s in STEPS[:STEPS.index(("gram", 0))] if s in FILLS)


def bank_number(fill):
    return fill % 4 if fill < EARLY else fill % 2


def on_act(step):
    return step[0] == "pick" or step[2] in ((1, 3) if step[1] == 0 else (0, 2))


def evicted(step):
    return sum(1 for s in FILLS[:FILLS.index(step) + 1] if on_act(s) == on_act(step))


def turned_at(step):
    return sum(1 for s in FILLS[:FILLS.index(step) + 1] if s[0] == "turn")


def build(nc, ids, ids_t, tables, feature, ctx_t, w1, b1, w2, b2, w3, out):
    with ExitStack() as stack:
        def sbuf(name, shape, dt=FP32):
            return stack.enter_context(nc.sbuf_tensor(name, shape, dt))

        def psum(name, shape):
            return stack.enter_context(nc.psum_tensor(name, shape, FP32))

        def sem(name):
            return stack.enter_context(nc.semaphore(name))

        picked = [tables[feature[pos]] for pos in range(N_PICK)]
        blocks = [-(-t.shape[0] // P) for t in picked]
        parts = [t.shape[0] // b for t, b in zip(picked, blocks)]
        assert all(p * b == t.shape[0] for p, b, t in zip(parts, blocks, picked))
        first_block = [sum(blocks[:i]) for i in range(N_PICK + 1)]
        max_blocks = max(blocks)
        spread = P - 16

        idx = sbuf("idx", [P, CH, F], INT32)
        ids_all = sbuf("ids_all", [P, N_PICK, B], INT32)
        row_of = {b: sbuf(f"row_of_{b}", [P, b]) for b in sorted(set(blocks))}
        minus_row = {b: sbuf(f"minus_row_{b}", [P, b]) for b in sorted(set(blocks))}
        table = sbuf("table", [P, TABLES, max_blocks, D])
        table_hi = sbuf("table_hi", [P, SPLITS, max_blocks, D], FP32R)
        table_lo = sbuf("table_lo", [P, SPLITS, max_blocks, D], FP32R)
        hot = sbuf("hot", [P, RING, B], FP32R)
        distance = sbuf("distance", [P, ACT_HOT, B])
        ident = sbuf("ident", [P, P])
        rows = sbuf("rows", [P, ROW_CHUNKS, len(GATHER_POS), D])
        emb = sbuf("emb", [P, CH, NQ, NS, FP])
        z = sbuf("z", [P, KT, B])
        w1s = sbuf("w1s", [P, KT, H1])
        w2s = sbuf("w2s", [P, J1, H2])
        w3s = sbuf("w3s", [P, J2])
        b1s = sbuf("b1s", [P, J1])
        b2s = sbuf("b2s", [P, J2])
        h1 = sbuf("h1", [P, 2, J1, P])
        h2 = sbuf("h2", [P, 2, J2, P])
        y = sbuf("y", [1, B])

        turn_bank = [psum(f"turn_bank_{i}", [P, GF, P]) for i in range(2)]
        gram = psum("gram", [P, 2 * GB, 512])
        hidden = [psum(f"hidden_{i}", [P, 4, P]) for i in range(2)]

        def l1_part(c, j):
            if c == CH - 1:
                return (hidden + turn_bank)[j][:, 0, :]
            return hidden[j // 2][:, j % 2, :]

        l1_ends = [(c, j) for c in range(CH) for j in range(J1) if c == CH - 1 or j % 2 == 1]

        def bank_of(fill):
            return (turn_bank + hidden)[bank_number(fill)]

        ids_in = sem("ids_in")
        ids_all_in = [sem(f"ids_all_in_{part}") for part in range(len(IDS_PARTS))]
        table_in = [sem(f"table_in_{i}") for i in range(TABLES)]
        gathered = [[sem(f"gathered_{c}_{k}") for k in range(len(GROUPS))] for c in range(CH)]
        rows_numbered = sem("rows_numbered")
        rows_negated = sem("rows_negated")
        ident_zeroed = sem("ident_zeroed")
        ident_made = sem("ident_made")
        emb_zeroed = sem("emb_zeroed")
        repeated = sem("repeated")
        z_zeroed = sem("z_zeroed")
        right_dve = sem("right_dve")
        right_act = sem("right_act")
        sample_1_left = sem("sample_1_left")
        hi_written = sem("hi_written")
        lo_written = sem("lo_written")
        hot_dve = sem("hot_dve")
        hot_act = sem("hot_act")
        distance_written = sem("distance_written")
        hot_used = sem("hot_used")
        weights_in = sem("weights_in")
        turned = sem("turned")
        emb_act = sem("emb_act")
        emb_dve = sem("emb_dve")
        gram_done = sem("gram_done")
        z_dve = sem("z_dve")
        z_act = sem("z_act")
        l1_done = sem("l1_done")
        h1_written = sem("h1_written")
        l2_done = sem("l2_done")
        h2_written = sem("h2_written")
        l3_done = sem("l3_done")
        y_written = sem("y_written")
        out_stored = sem("out_stored")
        n_weight_dmas = 5 + len(CTX_AT)
        block = stack.enter_context(nc.Block())

        def ids_part(i):
            return next(k for k, (a, e) in enumerate(IDS_PARTS) if a <= i < e)

        def act_blocks(i):
            return range(blocks[i] - ACT_HOT, blocks[i])

        def hot_slot(i, k):
            return (first_block[i] + k) % RING

        def evict_turn(engine, copy, step):
            _, c, k = step
            group = GROUPS[k]
            engine.wait_ge(turned, turned_at(step))
            return copy(emb[:, c, :, :, group[0]:group[-1] + 1],
                        bank_of(FILLS.index(step))[:, 0:len(group), :].rearrange("p f (s q) -> p q s f", s=NS))

        def move(copy, i, s, rows_and_columns):
            c, part = divmod(i, GRAMS_OF_CHUNK)
            bank, col = (i % 2) * GB, c * P + part * STEP_Q + s * NQ
            for g, rows, columns in rows_and_columns:
                src = gram[32 * s:32 * s + rows, bank:bank + GB, 0:BANK_COLS].rearrange(
                    "p k (q s n) -> p k q s n", q=BANK_Q, s=NS)[:, :, :, s, columns[0]:columns[-1] + 1:columns.step]
                dst = z[32 * g:32 * g + rows, :, col:col + STEP_Q]
                last = copy(dst.rearrange("p t (k q) -> p k q t", k=GB), src)
            return last

        RIGHT = [(g, ROWS[g], right) for g, (_, _, right) in enumerate(SLOTS)]
        LEFT = [(g, split, left) for g, (split, left, _) in enumerate(SLOTS)]

        @block.sync
        def _(sp):
            def load_table(i):
                if i >= TABLES:
                    sp.wait_ge(lo_written, i - TABLES + 1)
                view = picked[i].rearrange("(p b) d -> p b d", b=blocks[i])
                for a, e in ((0, spread), (spread, parts[i])):
                    sp.dma_start(table[a:e, i % TABLES, 0:blocks[i], :], view[a:e, :, :]).then_inc(table_in[i % TABLES], 16)

            def load_ids(part):
                a, e = IDS_PARTS[part]
                sp.dma_start(ids_all[:, a:e, :].rearrange("p i b -> p (i b)"),
                             ids_t[0:1, a * B:e * B].to_broadcast([P, (e - a) * B])).then_inc(ids_all_in[part], 16)

            sp.dma_start(idx[:, :, :], ids.rearrange("(c p) f -> p c f", p=P)).then_inc(ids_in, 16)
            for i in range(N_PICK):
                if i < len(IDS_PARTS):
                    load_ids(i)
                load_table(i)
            sp.dma_start(w1s[:, :, :], w1).then_inc(weights_in, 16)
            sp.dma_start(w2s[:, :, :], w2.rearrange("(t p) n -> p t n", p=P)).then_inc(weights_in, 16)
            sp.dma_start(w3s[:, :], w3).then_inc(weights_in, 16)
            sp.dma_start(b1s[:, :], b1).then_inc(weights_in, 16)
            sp.dma_start(b2s[:, :], b2).then_inc(weights_in, 16)
            sp.wait_ge(z_zeroed, 1)
            for row, k, part, t in CTX_AT:
                sp.dma_start(z[part:part + k, t, :], ctx_t[row:row + k, :]).then_inc(weights_in, 16)
            sp.wait_ge(y_written, CH)
            sp.dma_start(out, y[:, :]).then_inc(out_stored, 16)
            sp.wait_ge(out_stored, 16)

        @block.gpsimd
        def _(pool):
            for b in row_of:
                nc.gpsimd.iota(row_of[b][:, :], pattern=[[1, b]], base=0, channel_multiplier=b,
                               allow_small_or_imprecise_dtypes=True).then_inc(rows_numbered, 1)
            nc.gpsimd.memset(ident[:, :], 0.0).then_inc(ident_zeroed, 1)
            pool.wait_ge(ident_zeroed, 1)
            nc.gpsimd.affine_select(out=ident[:, :], in_=ident[:, :], compare_op=ALU.not_equal, fill=1.0,
                                    base=0, pattern=[[-1, P]], channel_multiplier=1).then_inc(ident_made, 1)
            pool.wait_ge(ids_in, 16)
            for c in range(CH):
                for k, group in enumerate(GROUPS):
                    if c >= ROW_CHUNKS:
                        pool.wait_ge(turned, turned_at(("turn", c - ROW_CHUNKS, k)))
                    for pos in group:
                        f = feature[pos]
                        pool.indirect_dma_start(
                            out=rows[:, c % ROW_CHUNKS, pos - N_PICK, :], out_offset=None, in_=tables[f][:, :],
                            in_offset=bass.IndirectOffsetOnAxis(ap=idx[:, c, f:f + 1], axis=0),
                        ).then_inc(gathered[c][k], 16)

        @block.vector
        def _(dve):
            def make_hot(i):
                dve.wait_ge(ids_all_in[ids_part(i)], 16)
                n = parts[i]
                for k in range(blocks[i]):
                    if k in act_blocks(i):
                        continue
                    if first_block[i] + k >= RING:
                        dve.wait_ge(hot_used, first_block[i] + k - RING + 1)
                    nc.vector.tensor_scalar(hot[0:n, hot_slot(i, k), :], ids_all[0:n, i, :],
                                            row_of[blocks[i]][0:n, k:k + 1], None, ALU.is_equal).then_inc(hot_dve, 1)

            def split_low(i):
                n = parts[i]
                dve.wait_ge(hi_written, i + 1)
                if i >= SPLITS:
                    dve.wait_ge(hot_used, first_block[i - SPLITS + 1])
                nc.vector.tensor_tensor(table_lo[0:n, i % SPLITS, 0:blocks[i], :], table[0:n, i % TABLES, 0:blocks[i], :],
                                        table_hi[0:n, i % SPLITS, 0:blocks[i], :].bitcast(FP32),
                                        ALU.subtract).then_inc(lo_written, 1)

            def repeat(c):
                if c == 0:
                    dve.wait_ge(emb_act, evicted(("pick", REPEATED[-1])))
                nc.vector.tensor_copy(emb[:, c, :, :, F:FR],
                                      emb[:, c, :, :, REPEATED[0]:REPEATED[-1] + 1]).then_inc(repeated, 1)

            nc.vector.memset(emb[:, :, :, :, FR:FP].rearrange("p c q s f -> p (c q s) f"), 0.0).then_inc(emb_zeroed, 1)
            nc.vector.memset(z[:, :, :], 0.0).then_inc(z_zeroed, 1)
            dve.wait_ge(rows_numbered, len(row_of))
            for i in range(LEAD):
                make_hot(i)
                split_low(i)
            for step in STEPS:
                if step[0] == "pick":
                    i = step[1]
                    if i + LEAD < N_PICK:
                        make_hot(i + LEAD)
                        split_low(i + LEAD)
                    if i == N_PICK - 1:
                        repeat(0)
                elif step[0] == "turn" and not on_act(step):
                    evict_turn(dve, nc.vector.tensor_copy, step).then_inc(emb_dve, 1)
                elif step[0] == "gram":
                    if step[1] == 0:
                        dve.wait_ge(z_zeroed, 1)
                    dve.wait_ge(gram_done, step[1] + 1)
                    i = step[1]
                    move(nc.vector.tensor_copy, i, 1, RIGHT).then_inc(right_dve, 1)
                    move(nc.vector.tensor_copy, i, 0, RIGHT).then_inc(right_dve, 1)
                    dve.wait_ge(right_dve, 2 * i + 1)
                    move(nc.vector.tensor_copy, i, 1, LEFT[:2]).then_inc(sample_1_left, 1)
                    dve.wait_ge(right_dve, 2 * i + 2)
                    move(nc.vector.tensor_copy, i, 0, LEFT).then_inc(z_dve, 1)
                    c, part = divmod(step[1], GRAMS_OF_CHUNK)
                    if part == 0 and c + 1 < CH:
                        repeat(c + 1)

        @block.scalar
        def _(act):
            def split_high(i):
                n = parts[i]
                act.wait_ge(table_in[i % TABLES], 32 * (i // TABLES + 1))
                if i >= SPLITS:
                    act.wait_ge(hot_used, first_block[i - SPLITS + 1])
                nc.scalar.copy(table_hi[0:n, i % SPLITS, 0:blocks[i], :], table[0:n, i % TABLES, 0:blocks[i], :]).then_inc(
                    hi_written, 1)

            def measure(i):
                n = parts[i]
                act.wait_ge(ids_all_in[ids_part(i)], 16)
                for d, k in enumerate(act_blocks(i)):
                    if i >= 1:
                        act.wait_ge(hot_act, ACT_HOT * (i - 1) + d + 1)
                    nc.scalar.activation(distance[0:n, d, :], ids_all[0:n, i, :], ACT.Abs,
                                         bias=minus_row[blocks[i]][0:n, k:k + 1]).then_inc(distance_written, 1)

            def make_hot(i):
                n = parts[i]
                for d, k in enumerate(act_blocks(i)):
                    if first_block[i] + k >= RING:
                        act.wait_ge(hot_used, first_block[i] + k - RING + 1)
                    act.wait_ge(distance_written, ACT_HOT * i + d + 1)
                    nc.scalar.activation(hot[0:n, hot_slot(i, k), :], distance[0:n, d, :], ACT.Relu,
                                         bias=1.0, scale=-1.0).then_inc(hot_act, 1)

            act.wait_ge(rows_numbered, len(row_of))
            for b in row_of:
                nc.scalar.mul(minus_row[b][:, :], row_of[b][:, :], -1.0).then_inc(rows_negated, 1)
            act.wait_ge(rows_negated, len(row_of))
            measure(0)
            split_high(0)
            make_hot(0)
            for i in range(1, LEAD):
                split_high(i)
                measure(i)
                make_hot(i)
            split_high(LEAD)
            for step in STEPS:
                if step[0] == "pick":
                    i = step[1]
                    fill = FILLS.index(step)
                    act.wait_ge(hot_used, first_block[i + 1])
                    nc.scalar.copy(
                        emb[:, :, :, :, i],
                        bank_of(fill)[:, :, :].rearrange("p c (s q) -> p c q s", s=NS)).then_inc(emb_act, 1)
                    if i + LEAD < N_PICK:
                        measure(i + LEAD)
                        make_hot(i + LEAD)
                    if i + LEAD + 1 < N_PICK:
                        split_high(i + LEAD + 1)
                elif step[0] == "turn" and on_act(step):
                    evict_turn(act, nc.scalar.copy, step).then_inc(emb_act, 1)
                elif step[0] == "gram":
                    if step[1] == 0:
                        act.wait_ge(z_zeroed, 1)
                    act.wait_ge(gram_done, step[1] + 1)
                    i = step[1]
                    move(nc.scalar.copy, i, 2, RIGHT).then_inc(right_act, 1)
                    move(nc.scalar.copy, i, 3, RIGHT).then_inc(right_act, 1)
                    act.wait_ge(right_act, 2 * i + 1)
                    move(nc.scalar.copy, i, 2, LEFT)
                    act.wait_ge(right_act, 2 * i + 2)
                    move(nc.scalar.copy, i, 3, LEFT)
                    act.wait_ge(sample_1_left, i + 1)
                    move(nc.scalar.copy, i, 1, LEFT[2:]).then_inc(z_act, 1)
                elif step[0] == "layer1":
                    c = step[1]
                    if c == 0:
                        act.wait_ge(weights_in, 16 * n_weight_dmas)
                    for j in range(J1):
                        if (c, j) in l1_ends:
                            act.wait_ge(l1_done, l1_ends.index((c, j)) + 1)
                        elif (c, j + 1) in l1_ends:
                            act.wait_ge(l1_done, l1_ends.index((c, j + 1)) + 1)
                        nc.scalar.activation(h1[:, c % 2, j, :], l1_part(c, j), ACT.Relu,
                                             bias=b1s[:, j:j + 1]).then_inc(h1_written, 1)
                elif step[0] == "layer2":
                    c = step[1]
                    for j in range(J2):
                        act.wait_ge(l2_done, 2 * c + j + 1)
                        nc.scalar.activation(h2[:, c % 2, j, :], hidden[j][:, 2, :], ACT.Relu,
                                             bias=b2s[:, j:j + 1]).then_inc(h2_written, 1)
                elif step[0] == "layer3":
                    c = step[1]
                    act.wait_ge(l3_done, c + 1)
                    nc.scalar.copy(y[:, c * P:(c + 1) * P], hidden[0][0:1, 3, :]).then_inc(y_written, 1)

        @block.tensor
        def _(pe):
            def wait_bank(fill):
                others = [f for f in range(fill) if bank_number(f) == bank_number(fill)]
                if others:
                    before = FILLS[others[-1]]
                    pe.wait_ge(emb_act if on_act(before) else emb_dve, evicted(before))

            pe.wait_ge(ident_made, 1)
            for step in STEPS:
                if step[0] == "pick":
                    i = step[1]
                    fill = FILLS.index(step)
                    wait_bank(fill)
                    pe.wait_ge(hi_written, i + 1)
                    n = parts[i]
                    bank = bank_of(fill)[:, :, :].rearrange("p c s -> p (c s)")
                    dve_blocks = blocks[i] - ACT_HOT
                    for k in range(blocks[i]):
                        if k in act_blocks(i):
                            pe.wait_ge(hot_act, ACT_HOT * i + k - dve_blocks + 1)
                        else:
                            pe.wait_ge(hot_dve, first_block[i] - ACT_HOT * i + k + 1)
                        nc.tensor.matmul(bank, table_hi[0:n, i % SPLITS, k, :], hot[0:n, hot_slot(i, k), :],
                                         start=(k == 0), stop=False)
                    pe.wait_ge(lo_written, i + 1)
                    for k in range(blocks[i]):
                        last = nc.tensor.matmul(bank, table_lo[0:n, i % SPLITS, k, :], hot[0:n, hot_slot(i, k), :],
                                                start=False, stop=(k == blocks[i] - 1))
                        last.then_inc(hot_used, 1)
                elif step[0] == "turn":
                    _, c, k = step
                    group = GROUPS[k]
                    fill = FILLS.index(step)
                    wait_bank(fill)
                    pe.wait_ge(gathered[c][k], 16 * len(group))
                    for pos in group:
                        last = nc.tensor.transpose(bank_of(fill)[:, pos - group[0], :],
                                                   rows[:, c % ROW_CHUNKS, pos - N_PICK, :], ident[:, :])
                    last.then_inc(turned, 1)
                elif step[0] == "gram":
                    i = step[1]
                    c, part = divmod(i, GRAMS_OF_CHUNK)
                    if i == 0:
                        pe.wait_ge(emb_zeroed, 1)
                    if i >= 2:
                        pe.wait_ge(z_dve, i - 1)
                        pe.wait_ge(z_act, i - 1)
                    if part == 0:
                        pe.wait_ge(repeated, c + 1)
                        own = [s for s in FILLS if s[0] == "pick" or s[1] == c]
                        pe.wait_ge(emb_act, max(evicted(s) for s in own if on_act(s)))
                        pe.wait_ge(emb_dve, max(evicted(s) for s in own if not on_act(s)))
                    for k in range(GB):
                        for qq in range(BANK_Q):
                            q = part * STEP_Q + k * BANK_Q + qq
                            last = nc.tensor.matmul(
                                gram[0:M_GRAM, (i % 2) * GB + k, qq * NS * F:(qq + 1) * NS * F],
                                emb[:, c, q, :, :].rearrange("p s f -> p (s f)")[:, 0:M_GRAM],
                                emb[:, c, q, :, 0:F], start=True, stop=True)
                    last.then_inc(gram_done, 1)
                elif step[0] == "layer1":
                    c = step[1]
                    cols = slice(c * P, (c + 1) * P)
                    if c == 0:
                        pe.wait_ge(weights_in, 16 * n_weight_dmas)
                    else:
                        pe.wait_ge(y_written, c)
                    pe.wait_ge(z_dve, GRAMS_OF_CHUNK * (c + 1))
                    pe.wait_ge(z_act, GRAMS_OF_CHUNK * (c + 1))
                    for j in range(J1):
                        for t in range(KT):
                            last = nc.tensor.matmul(l1_part(c, j), w1s[:, t, j * P:(j + 1) * P],
                                                    z[:, t, cols], start=(t == 0), stop=(t == KT - 1))
                        if (c, j) in l1_ends:
                            last.then_inc(l1_done, 1)
                elif step[0] == "layer2":
                    c = step[1]
                    for j in range(J2):
                        for t in range(J1):
                            if j == 0:
                                pe.wait_ge(h1_written, J1 * c + (t + 1 if c == CH - 1 else max(t + 1, 2)))
                            last = nc.tensor.matmul(hidden[j][:, 2, :], w2s[:, t, j * P:(j + 1) * P],
                                                    h1[:, c % 2, t, :], start=(t == 0), stop=(t == J1 - 1))
                        last.then_inc(l2_done, 1)
                elif step[0] == "layer3":
                    c = step[1]
                    for t in range(J2):
                        pe.wait_ge(h2_written, J2 * c + t + 1)
                        last = nc.tensor.matmul(hidden[0][0:1, 3, :], w3s[:, t:t + 1],
                                                h2[:, c % 2, t, :], start=(t == 0), stop=(t == J2 - 1))
                    last.then_inc(l3_done, 1)


def kernel(**inputs):
    import numpy as _np
    import concourse.bacc as _bacc
    from concourse import mybir as _mybir
    from concourse.bass_utils import run_bass_kernel_spmd as _run

    nc = _bacc.Bacc("TRN2", target_bir_lowering=False, num_devices=1)
    arrays = {}

    def dram(name, a):
        a = _np.ascontiguousarray(a)
        arrays[f"in_{name}_dram"] = a
        return nc.dram_tensor(f"in_{name}_dram", a.shape, _mybir.dt.from_np(a.dtype), kind="ExternalInput").ap()

    ids = dram("ids", inputs["ids"])
    tables = [dram(f"tbl_{f}", inputs[f"tbl_{f}"]) for f in range(F)]
    feature = plan_features([t.shape[0] for t in tables])
    ids_t = dram("ids_t", _np.asarray(inputs["ids"]).T[[feature[pos] for pos in range(N_PICK)]].reshape(1, N_PICK * B))
    ctx_t = dram("ctx_t", _np.asarray(inputs["dense_ctx"]).T)
    w_top1 = _np.asarray(inputs["W_top1"])
    w1_rows = _np.zeros((P, KT, H1), w_top1.dtype)
    first_pair = [f * (F - 1) - f * (f - 1) // 2 - f - 1 for f in range(F)]
    for (m, n), (part, t) in PAIR_AT.items():
        a, b = sorted((feature[m], feature[n]))
        w1_rows[part, t] = w_top1[first_pair[a] + b]
    for row, k, part, t in CTX_AT:
        w1_rows[part:part + k, t] = w_top1[NPAIR + row:NPAIR + row + k]
    w1 = dram("W_top1", w1_rows)
    b1 = dram("b_top1", _np.asarray(inputs["b_top1"]).reshape(J1, P).T)
    w2 = dram("W_top2", inputs["W_top2"])
    b2 = dram("b_top2", _np.asarray(inputs["b_top2"]).reshape(J2, P).T)
    w3 = dram("W_top3", _np.asarray(inputs["W_top3"]).reshape(J2, P).T)
    out = nc.dram_tensor("out_0_dram", (1, B), FP32, kind="ExternalOutput").ap()
    build(nc, ids, ids_t, tables, feature, ctx_t, w1, b1, w2, b2, w3, out)
    r = _run(nc, [arrays], core_ids=[0])
    return _np.asarray(r.results[0]["out_0_dram"]).reshape(B, 1)
```
